# Optimizing a Trainium2 kernel written in Bass

```python
import numpy as np
import jax
import jax.numpy as jnp

def _softmax(x, axis=-1):
    return jax.nn.softmax(x, axis=axis)

def _gelu(x):
    return jax.nn.gelu(x, approximate=True)

def _silu(x):
    return jax.nn.silu(x)

def _sigmoid(x):
    return jax.nn.sigmoid(x)

def _layernorm(x, axis=-1, eps=1e-05):
    m = jnp.mean(x, axis=axis, keepdims=True)
    v = jnp.var(x, axis=axis, keepdims=True)
    return (x - m) / jnp.sqrt(v + eps)

def _scatter_add(tgt, idx, src, axis=0):
    return tgt.at[idx].add(src)

def _segment_sum(src, seg, n):
    return jax.ops.segment_sum(src, seg, n)
kernel_name = 'mk_rec_standalone_d1_rec_r8_4dcdac'

def setup_inputs(seed: int=0):
    np.random.seed(seed)
    _w = jnp.asarray

    def _rec_inputs():
        import jax
        import jax.numpy as jnp
        _rk = jax.random.key(seed)
        r_white_features = jax.random.uniform(jax.random.fold_in(_rk, 1), (512, 5120), jnp.float32, 0.0, 1)
        r_black_features = jax.random.uniform(jax.random.fold_in(_rk, 2), (512, 5120), jnp.float32, 0.0, 1)
        r_side_to_move = jnp.ones((512,), jnp.float32)
        return (r_white_features, r_black_features, r_side_to_move)
    r_white_features, r_black_features, r_side_to_move = _rec_inputs()

    def _L0_rec_setup():
        import jax, jax.numpy as jnp
        import numpy as np
        B = 512
        IN = 5120
        H = 256
        key = jax.random.key(seed)
        ks = jax.random.split(key, 10)
        white_features = jax.random.uniform(ks[0], (B, IN), dtype=jnp.float32)
        black_features = jax.random.uniform(ks[1], (B, IN), dtype=jnp.float32)
        side_to_move = jnp.ones((B,), dtype=jnp.float32)
        W_ft = 0.1 * jax.random.normal(ks[2], (H, IN), dtype=jnp.float32)

        def xavier(k, shape):
            fan_out, fan_in = shape
            std = float(np.sqrt(2.0 / (fan_in + fan_out)))
            return std * jax.random.normal(k, shape, dtype=jnp.float32)
        W1 = xavier(ks[3], (32, 2 * H))
        b1 = jnp.zeros((32,), jnp.float32)
        W2 = xavier(ks[4], (32, 32))
        b2 = jnp.zeros((32,), jnp.float32)
        W3 = xavier(ks[5], (1, 32))
        b3 = jnp.zeros((1,), jnp.float32)
        return {'white_features': white_features, 'black_features': black_features, 'side_to_move': side_to_move, 'W_ft': W_ft, 'W1': W1, 'b1': b1, 'W2': W2, 'b2': b2, 'W3': W3, 'b3': b3}
    _L0_rec_all = _L0_rec_setup()
    _L0_rec_in = {k: v for k, v in _L0_rec_all.items() if k in ('W_ft', 'W1', 'b1', 'W2', 'b2', 'W3', 'b3')}
    del _L0_rec_all
    return {'r_white_features': r_white_features, 'r_black_features': r_black_features, 'r_side_to_move': r_side_to_move, 'L0_rec_W_ft': _L0_rec_in['W_ft'], 'L0_rec_W1': _L0_rec_in['W1'], 'L0_rec_b1': _L0_rec_in['b1'], 'L0_rec_W2': _L0_rec_in['W2'], 'L0_rec_b2': _L0_rec_in['b2'], 'L0_rec_W3': _L0_rec_in['W3'], 'L0_rec_b3': _L0_rec_in['b3']}

def reference(r_white_features, r_black_features, r_side_to_move, L0_rec_W_ft, L0_rec_W1, L0_rec_b1, L0_rec_W2, L0_rec_b2, L0_rec_W3, L0_rec_b3):
    import jax
    import jax.numpy as jnp

    def _L0_rec_ref(white_features, black_features, side_to_move, W_ft, W1, b1, W2, b2, W3, b3):
        import jax, jax.numpy as jnp
        import numpy as np
        B = 512
        IN = 5120
        H = 256
        wh = jnp.clip(white_features @ W_ft.T, 0.0, 1.0)
        bh = jnp.clip(black_features @ W_ft.T, 0.0, 1.0)
        x = jnp.concatenate([wh, bh], axis=1)
        x = jax.nn.relu(x @ W1.T + b1)
        x = jax.nn.relu(x @ W2.T + b2)
        evaluation = x @ W3.T + b3
        return evaluation * side_to_move[:, None]
    y = _L0_rec_ref(r_white_features, r_black_features, r_side_to_move, L0_rec_W_ft, L0_rec_W1, L0_rec_b1, L0_rec_W2, L0_rec_b2, L0_rec_W3, L0_rec_b3)
    return y

_drawn_inputs = setup_inputs


def setup_inputs(seed=0):
    import zlib

    import numpy as np

    out = dict(_drawn_inputs(seed))
    spreads = {'r_side_to_move': (1.0, 0.2), 'L0_rec_b1': (0.0, 0.1), 'L0_rec_b2': (0.0, 0.1)}
    factors = {}
    for name, (base, spread) in spreads.items():
        noise = np.random.default_rng([zlib.crc32(name.encode()), seed]).standard_normal(out[name].shape)
        drawn = base * np.exp(spread * noise) if base else spread * noise
        out[name] = jnp.asarray(drawn.astype(out[name].dtype))
    for name, factor in factors.items():
        out[name] = (out[name] * factor).astype(out[name].dtype)
    return out
```

```python
import concourse.bass as bass
from concourse import mybir
from contextlib import ExitStack

P = 128
BATCH = 512
IN = 5120
H = 256
L = 32
SIDES = 2
KT = IN // P
HB = H // P
ROW = H + SIDES * BATCH
RING = 8
TURNS = KT // RING
GROUPED = 4
HALF = BATCH // 2


def feature_net_kernel(
    nc: bass.Bass,
    packed: bass.AP,
    side_to_move: bass.AP,
    w1t: bass.AP,
    b1: bass.AP,
    w2t: bass.AP,
    b2: bass.AP,
    w3t: bass.AP,
    b3: bass.AP,
    out: bass.AP,
):
    f32 = mybir.dt.float32
    f32r = mybir.dt.float32r
    ALU = mybir.AluOpType
    ACT = mybir.ActivationFunctionType
    assert KT % RING == 0 and GROUPED <= RING

    packed_v = packed.rearrange("(p t) n -> p t n", t=KT)

    ctx = ExitStack()
    with ctx:
        def sb(name, shape, dt=f32):
            return ctx.enter_context(nc.sbuf_tensor(name, shape, dt))

        def bank(name):
            return ctx.enter_context(nc.psum_tensor(name, [P, BATCH], f32))

        def sem(name):
            return ctx.enter_context(nc.semaphore(name))

        raw = sb("raw", [P, RING, ROW])
        high = sb("high", [P, RING, ROW], f32r)
        low = sb("low", [P, RING, ROW], f32r)
        zeros = sb("zeros", [P, BATCH], f32)
        zeros_r = sb("zeros_r", [P, BATCH], f32r)
        clipped = sb("clipped", [P, SIDES * HB, BATCH])
        w1_sb = sb("w1_sb", [P, SIDES * HB, L])
        w2_sb = sb("w2_sb", [L, L])
        w3_sb = sb("w3_sb", [L, 1])
        b1_sb = sb("b1_sb", [L, 1])
        b2_sb = sb("b2_sb", [L, 1])
        b3_sb = sb("b3_sb", [1, 1])
        stm_sb = sb("stm_sb", [1, BATCH])
        l1_sb = sb("l1_sb", [L, BATCH])
        l2_sb = sb("l2_sb", [L, BATCH])
        out_sb = sb("out_sb", [1, BATCH])

        acc = [bank(f"acc{g}") for g in range(SIDES * HB)]
        l1_ps = [bank(f"l1_ps{c}") for c in range(2)]
        l2_ps = [bank(f"l2_ps{c}") for c in range(2)]
        l3_ps = [acc[0], acc[1]]

        raw_loaded = [sem(f"raw_loaded{s}") for s in range(RING)]
        high_ready = sem("high_ready")
        low_ready = sem("low_ready")
        tile_used = sem("tile_used")
        params_loaded = sem("params_loaded")
        zeros_set = sem("zeros_set")
        zeros_ready = sem("zeros_ready")
        group_done = sem("group_done")
        clip_done = sem("clip_done")
        l1_done = sem("l1_done")
        l1_relu = sem("l1_relu")
        l2_done = sem("l2_done")
        l2_relu = sem("l2_relu")
        l3_done = sem("l3_done")
        row_done = sem("row_done")
        out_stored = sem("out_stored")
        block = ctx.enter_context(nc.Block())

        def half(c):
            return slice(c * HALF, (c + 1) * HALF)

        @block.sync
        def _(sync):
            for s in range(RING):
                sync.dma_start(raw[:, s, :], packed_v[:, s, :]).then_inc(raw_loaded[s], 16)
            params = [(w1_sb[:, :, :], w1t.rearrange("(g p) j -> p g j", p=P)), (w2_sb[:, :], w2t),
                      (w3_sb[:, :], w3t), (b1_sb[:, :], b1), (b2_sb[:, :], b2), (b3_sb[:, :], b3),
                      (stm_sb[:, :], side_to_move)]
            for dst, src in params:
                sync.dma_start(dst, src).then_inc(params_loaded, 16)
            with sync.Fori(1, TURNS) as turn:
                for s in range(RING):
                    sync.wait_ge(low_ready, (turn - 1) * RING + s + 1)
                    sync.dma_start(raw[:, s, :],
                                   packed_v[:, bass.ds(turn * RING + s, 1), :].rearrange("p t n -> p (t n)")
                                   ).then_inc(raw_loaded[s], 16)
            sync.wait_ge(row_done, 2)
            sync.dma_start(out, out_sb[:, :]).then_inc(out_stored, 16)
            sync.wait_ge(out_stored, 16)

        @block.gpsimd
        def _(gpsimd):
            nc.gpsimd.memset(zeros[:, :], 0.0).then_inc(zeros_set, 1)

        @block.scalar
        def _(act):
            act.wait_ge(zeros_set, 1)
            nc.scalar.activation(zeros_r[:, :], zeros[:, :], ACT.Copy).then_inc(zeros_ready, 1)

            for s in range(RING):
                act.wait_ge(raw_loaded[s], 16)
                nc.scalar.activation(high[:, s, :], raw[:, s, :], ACT.Copy).then_inc(high_ready, 1)
            with act.Fori(1, TURNS) as turn:
                for s in range(RING):
                    act.wait_ge(raw_loaded[s], 16 * (turn + 1))
                    act.wait_ge(tile_used, (turn - 1) * RING + s + 1)
                    nc.scalar.activation(high[:, s, :], raw[:, s, :], ACT.Copy).then_inc(high_ready, 1)

            act.wait_ge(params_loaded, 16 * 7)
            for c in range(2):
                act.wait_ge(l1_done, c + 1)
                nc.scalar.activation(l1_sb[:, half(c)], l1_ps[c][0:L, 0:HALF], ACT.Relu,
                                     bias=b1_sb[:, :]).then_inc(l1_relu, 1)

        @block.vector
        def _(dve):
            def split_low(s):
                nc.vector.tensor_tensor(low[:, s, :], raw[:, s, :], high[:, s, :].bitcast(f32),
                                        ALU.subtract).then_inc(low_ready, 1)

            for s in range(RING):
                dve.wait_ge(high_ready, s + 1)
                split_low(s)
            with dve.Fori(1, TURNS) as turn:
                for s in range(RING):
                    dve.wait_ge(high_ready, turn * RING + s + 1)
                    split_low(s)

            dve.wait_ge(params_loaded, 16 * 7)
            for g in range(SIDES * HB):
                dve.wait_ge(group_done, g + 1)
                for c in range(2):
                    nc.vector.tensor_scalar(clipped[:, g, half(c)], acc[g][:, half(c)], 0.0, 1.0,
                                            ALU.max, ALU.min).then_inc(clip_done, 1)
            for c in range(2):
                dve.wait_ge(l2_done, c + 1)
                nc.vector.tensor_scalar(l2_sb[:, half(c)], l2_ps[c][0:L, 0:HALF], b2_sb[:, :], 0.0,
                                        ALU.add, ALU.max).then_inc(l2_relu, 1)
            for c in range(2):
                dve.wait_ge(l3_done, c + 1)
                nc.vector.scalar_tensor_tensor(out=out_sb[:, half(c)], in0=l3_ps[c][0:1, 0:HALF],
                                               scalar=b3_sb[:, :], in1=stm_sb[:, half(c)],
                                               op0=ALU.add, op1=ALU.mult).then_inc(row_done, 1)

        @block.tensor
        def _(pe):
            pe.wait_ge(zeros_ready, 1)
            for g in range(SIDES * HB):
                nc.tensor.matmul(acc[g][:, :], zeros_r[:, 0:P], zeros_r[:, :], start=True, stop=False)

            def product(s, g, w, x, stop=False):
                side, hb = g // HB, g % HB
                return nc.tensor.matmul(acc[g][:, :], w[:, s, hb * P:(hb + 1) * P],
                                        x[:, s, H + side * BATCH:H + (side + 1) * BATCH],
                                        start=False, stop=stop)

            def tile(s):
                for hb in range(HB):
                    for x in (high, low):
                        for side in range(SIDES):
                            product(s, side * HB + hb, high, x)
                    for side in range(SIDES):
                        last = product(s, side * HB + hb, low, high)
                last.then_inc(tile_used, 1)

            with pe.Fori(0, TURNS - 1) as turn:
                for s in range(RING):
                    pe.wait_ge(low_ready, turn * RING + s + 1)
                    tile(s)
            for s in range(RING - GROUPED):
                pe.wait_ge(low_ready, KT - RING + s + 1)
                tile(s)
            pe.wait_ge(low_ready, KT)

            def layer1(g, c):
                return nc.tensor.matmul(l1_ps[c][0:L, 0:HALF], w1_sb[:, g, :], clipped[:, g, half(c)],
                                        start=(g == 0), stop=(g == SIDES * HB - 1))

            for g in range(SIDES * HB):
                for s in range(RING - GROUPED, RING):
                    product(s, g, high, high)
                    product(s, g, high, low)
                    last = product(s, g, low, high, stop=(s == RING - 1))
                last.then_inc(group_done, 1)
                if g >= 1:
                    pe.wait_ge(clip_done, 2 * g)
                    for c in range(2):
                        layer1(g - 1, c)
            for c in range(2):
                pe.wait_ge(clip_done, 2 * (SIDES * HB - 1) + c + 1)
                layer1(SIDES * HB - 1, c).then_inc(l1_done, 1)
            for c in range(2):
                pe.wait_ge(l1_relu, c + 1)
                nc.tensor.matmul(l2_ps[c][0:L, 0:HALF], w2_sb[:, :], l1_sb[:, half(c)],
                                 start=True, stop=True).then_inc(l2_done, 1)
            for c in range(2):
                pe.wait_ge(l2_relu, c + 1)
                nc.tensor.matmul(l3_ps[c][0:1, 0:HALF], w3_sb[:, :], l2_sb[:, half(c)],
                                 start=True, stop=True).then_inc(l3_done, 1)


def kernel(r_white_features, r_black_features, r_side_to_move, L0_rec_W_ft, L0_rec_W1, L0_rec_b1,
           L0_rec_W2, L0_rec_b2, L0_rec_W3, L0_rec_b3):
    import numpy as np
    import concourse.bacc as bacc
    from concourse.bass_utils import run_bass_kernel_spmd

    packed = np.concatenate([np.asarray(L0_rec_W_ft).T, np.asarray(r_white_features).T,
                             np.asarray(r_black_features).T], axis=1)
    laid = {
        "packed": packed,
        "side_to_move": np.asarray(r_side_to_move).reshape(1, BATCH),
        "w1t": np.asarray(L0_rec_W1).T,
        "b1": np.asarray(L0_rec_b1).reshape(L, 1),
        "w2t": np.asarray(L0_rec_W2).T,
        "b2": np.asarray(L0_rec_b2).reshape(L, 1),
        "w3t": np.asarray(L0_rec_W3).T,
        "b3": np.asarray(L0_rec_b3).reshape(1, 1),
    }
    nc = bacc.Bacc("TRN2", target_bir_lowering=False, num_devices=1)
    arrays, args = {}, []
    for name, a in laid.items():
        arrays[name] = np.ascontiguousarray(a)
        args.append(nc.dram_tensor(name, a.shape, mybir.dt.from_np(a.dtype), kind="ExternalInput").ap())
    out = nc.dram_tensor("out", (1, BATCH), mybir.dt.float32, kind="ExternalOutput").ap()
    feature_net_kernel(nc, *args, out)
    r = run_bass_kernel_spmd(nc, [arrays], core_ids=[0])
    return r.results[0]["out"].reshape(BATCH, 1)
```

```python
import concourse.bass as bass
from concourse import mybir
from contextlib import ExitStack

P = 128
BATCH = 512
IN = 5120
H = 256
L = 32
SIDES = 2
KT = IN // P
HB = H // P
ROW = H + SIDES * BATCH
RING = 8
TURNS = KT // RING
GROUPED = 4
QUARTERS = P // L
QUARTER = BATCH // QUARTERS
GROUPS = SIDES * HB
WAKE = 8

PIECES = [slice(0, H), slice(H, H + BATCH), slice(H + BATCH, ROW)]
PARTS = [slice(0, H), slice(H, ROW)]


def highs(t):
    return t + len(PIECES)


def lows(t):
    if isinstance(t, int) and t < RING:
        return len(PIECES) + len(PARTS) * t
    return t + len(PIECES) + len(PARTS) * (RING - 1) - (RING - 1)


def feature_net_kernel(
    nc: bass.Bass,
    packed: bass.AP,
    side_to_move: bass.AP,
    w1t: bass.AP,
    b1: bass.AP,
    w2t: bass.AP,
    b2: bass.AP,
    w3t: bass.AP,
    b3: bass.AP,
    out: bass.AP,
):
    f32 = mybir.dt.float32
    f32r = mybir.dt.float32r
    bf16 = mybir.dt.bfloat16
    ALU = mybir.AluOpType
    ACT = mybir.ActivationFunctionType
    assert KT % RING == 0 and GROUPED <= RING and TURNS >= 3

    packed_v = packed.rearrange("(p t) n -> p t n", t=KT)

    ctx = ExitStack()
    with ctx:
        def sb(name, shape, dt=f32):
            return ctx.enter_context(nc.sbuf_tensor(name, shape, dt))

        def bank(name):
            return ctx.enter_context(nc.psum_tensor(name, [P, BATCH], f32))

        def sem(name):
            return ctx.enter_context(nc.semaphore(name))

        raw = sb("raw", [P, RING, ROW])
        high = sb("high", [P, RING, ROW], f32r)
        low = sb("low", [P, RING, ROW], f32r)
        zeros = sb("zeros", [P, BATCH], bf16)
        clipped = sb("clipped", [P, GROUPS, BATCH])
        w1_sb = sb("w1_sb", [P, GROUPS, L])
        w2_diag = sb("w2_diag", [P, P])
        w3_diag = sb("w3_diag", [P, QUARTERS])
        b1_sb = sb("b1_sb", [P, 1])
        b2_sb = sb("b2_sb", [P, 1])
        b3_sb = sb("b3_sb", [QUARTERS, 1])
        stm_sb = sb("stm_sb", [QUARTERS, QUARTER])
        l1_sb = sb("l1_sb", [P, QUARTER])
        l2_sb = sb("l2_sb", [P, QUARTER])
        out_sb = sb("out_sb", [QUARTERS, QUARTER])

        acc = [bank(f"acc{g}") for g in range(GROUPS)]
        l1_ps = bank("l1_ps")
        l2_ps = bank("l2_ps")
        l3_ps = bank("l3_ps")

        piece_loaded = [sem(f"piece_loaded{i}") for i in range(len(PIECES))]
        raw_loaded = [sem(f"raw_loaded{s}") for s in range(RING)]
        high_ready = sem("high_ready")
        low_ready = sem("low_ready")
        tile_used = sem("tile_used")
        diag_zeroed = sem("diag_zeroed")
        params_loaded = sem("params_loaded")
        zeros_ready = sem("zeros_ready")
        group_done = sem("group_done")
        clip_done = sem("clip_done")
        l1_done = sem("l1_done")
        l1_relu = sem("l1_relu")
        l2_done = sem("l2_done")
        l2_relu = sem("l2_relu")
        l3_done = sem("l3_done")
        row_done = sem("row_done")
        out_stored = sem("out_stored")
        block = ctx.enter_context(nc.Block())

        def loads(s):
            return 0 if s == 0 else 16

        def quarter(q):
            return slice(q * QUARTER, (q + 1) * QUARTER)

        def parts(q):
            return slice(q * L, (q + 1) * L)

        @block.sync
        def _(sync):
            for i, cols in enumerate(PIECES):
                sync.dma_start(raw[:, 0, cols], packed_v[:, 0, cols]).then_inc(piece_loaded[i], 16)
            for s in range(1, RING):
                sync.dma_start(raw[:, s, :], packed_v[:, s, :]).then_inc(raw_loaded[s], 16)
            with sync.Fori(1, TURNS) as turn:
                for s in range(RING):
                    sync.wait_ge(low_ready, lows((turn - 1) * RING + s))
                    sync.dma_start(raw[:, s, :],
                                   packed_v[:, bass.ds(turn * RING + s, 1), :].rearrange("p t n -> p (t n)")
                                   ).then_inc(raw_loaded[s], 16)
            sync.wait_ge(row_done, 1)
            sync.dma_start(out, out_sb[:, :]).then_inc(out_stored, 16)
            sync.wait_ge(out_stored, 16)

        param_loads = [(w1_sb[:, :, :], w1t.rearrange("(g p) j -> p g j", p=P)),
                       (b3_sb[:, :], b3.to_broadcast([QUARTERS, 1])), (stm_sb[:, :], side_to_move)]
        for q in range(QUARTERS):
            param_loads += [(w2_diag[parts(q), parts(q)], w2t), (w3_diag[parts(q), q:q + 1], w3t),
                            (b1_sb[parts(q), :], b1), (b2_sb[parts(q), :], b2)]
        PARAMS = 16 * len(param_loads)

        @block.gpsimd
        def _(gpsimd):
            nc.gpsimd.memset(w2_diag[:, :], 0.0).then_inc(diag_zeroed, 1)
            nc.gpsimd.memset(w3_diag[:, :], 0.0).then_inc(diag_zeroed, 1)
            gpsimd.wait_ge(diag_zeroed, 2)
            for dst, src in param_loads:
                gpsimd.dma_start(dst, src).then_inc(params_loaded, 16)

        @block.scalar
        def _(act):
            def split_high(s, cols=slice(0, ROW)):
                nc.scalar.activation(high[:, s, cols], raw[:, s, cols], ACT.Copy).then_inc(high_ready, 1)

            for i, cols in enumerate(PIECES):
                act.wait_ge(piece_loaded[i], 16)
                split_high(0, cols)
            for s in range(1, RING):
                act.wait_ge(raw_loaded[s], loads(s))
                split_high(s)
            with act.Fori(1, TURNS) as turn:
                for s in range(RING):
                    act.wait_ge(raw_loaded[s], (turn - 1) * 16 + loads(s) + 16)
                    act.wait_ge(tile_used, (turn - 1) * RING + s + 1)
                    split_high(s)

        @block.vector
        def _(dve):
            def split_low(s, cols=slice(0, ROW)):
                nc.vector.tensor_tensor(low[:, s, cols], raw[:, s, cols], high[:, s, cols].bitcast(f32),
                                        ALU.subtract).then_inc(low_ready, 1)

            nc.vector.memset(zeros[:, :], 0.0).then_inc(zeros_ready, 1)
            for i, cols in enumerate(PIECES):
                dve.wait_ge(high_ready, i + 1)
                split_low(0, cols)
            for s in range(1, RING):
                dve.wait_ge(high_ready, highs(s))
                for cols in PARTS:
                    split_low(s, cols)
            with dve.Fori(1, TURNS) as turn:
                for s in range(RING):
                    dve.wait_ge(high_ready, highs(turn * RING + s))
                    split_low(s)

            for g in range(GROUPS):
                dve.wait_ge(group_done, g + 1)
                for q in range(QUARTERS):
                    nc.vector.tensor_scalar(clipped[:, g, quarter(q)], acc[g][:, quarter(q)], 0.0, 1.0,
                                            ALU.max, ALU.min).then_inc(clip_done, 1)
            dve.wait_ge(params_loaded, PARAMS)
            dve.wait_ge(l1_done, 1)
            nc.vector.tensor_scalar(l1_sb[:, :], l1_ps[:, 0:QUARTER], b1_sb[:, :], 0.0,
                                    ALU.add, ALU.max).then_inc(l1_relu, 1)
            dve.wait_ge(l2_done, 1)
            nc.vector.tensor_scalar(l2_sb[:, :], l2_ps[:, 0:QUARTER], b2_sb[:, :], 0.0,
                                    ALU.add, ALU.max).then_inc(l2_relu, 1)
            dve.wait_ge(l3_done, 1)
            nc.vector.scalar_tensor_tensor(out=out_sb[:, :], in0=l3_ps[0:QUARTERS, 0:QUARTER],
                                           scalar=b3_sb[:, :], in1=stm_sb[:, :],
                                           op0=ALU.add, op1=ALU.mult).then_inc(row_done, 1)

        @block.tensor
        def _(pe):
            pe.wait_ge(zeros_ready, 1)
            for _ in range(WAKE - GROUPS):
                nc.tensor.matmul(l3_ps[:, :], zeros[:, 0:P], zeros[:, :], start=True, stop=True)
            for g in range(GROUPS):
                nc.tensor.matmul(acc[g][:, :], zeros[:, 0:P], zeros[:, :], start=True, stop=False)

            def product(s, side, hb, w, x, stop=False):
                return nc.tensor.matmul(acc[side * HB + hb][:, :], w[:, s, hb * P:(hb + 1) * P],
                                        x[:, s, H + side * BATCH:H + (side + 1) * BATCH],
                                        start=False, stop=stop)

            for side in range(SIDES):
                pe.wait_ge(high_ready, 2 + side)
                for hb in range(HB):
                    product(0, side, hb, high, high)
            for i in range(len(PIECES)):
                pe.wait_ge(low_ready, i + 1)
                for hb in range(HB):
                    if i == 0:
                        for side in range(SIDES):
                            product(0, side, hb, low, high)
                    else:
                        last = product(0, i - 1, hb, high, low)
            last.then_inc(tile_used, 1)
            for s in range(1, RING):
                pe.wait_ge(high_ready, highs(s))
                for hb in range(HB):
                    for side in range(SIDES):
                        product(s, side, hb, high, high)
                pe.wait_ge(low_ready, lows(s) - 1)
                for hb in range(HB):
                    for side in range(SIDES):
                        product(s, side, hb, low, high)
                pe.wait_ge(low_ready, lows(s))
                for hb in range(HB):
                    for side in range(SIDES):
                        last = product(s, side, hb, high, low)
                last.then_inc(tile_used, 1)

            def tile(s):
                for hb in range(HB):
                    for x in (high, low):
                        for side in range(SIDES):
                            product(s, side, hb, high, x)
                    for side in range(SIDES):
                        last = product(s, side, hb, low, high)
                last.then_inc(tile_used, 1)

            with pe.Fori(1, TURNS - 1) as turn:
                for s in range(RING):
                    pe.wait_ge(low_ready, lows(turn * RING + s))
                    tile(s)
            for s in range(RING - GROUPED):
                pe.wait_ge(low_ready, lows(KT - RING + s))
                tile(s)

            def grouped(g):
                for s in range(RING - GROUPED, RING):
                    for w, x in ((high, high), (high, low), (low, high)):
                        last = product(s, g // HB, g % HB, w, x, stop=(w is low and s == RING - 1))
                last.then_inc(group_done, 1)

            def layer1(g):
                for q in range(QUARTERS):
                    pe.wait_ge(clip_done, g * QUARTERS + q + 1)
                    last = nc.tensor.matmul(l1_ps[parts(q), 0:QUARTER], w1_sb[:, g, :],
                                            clipped[:, g, quarter(q)],
                                            start=(g == 0), stop=(g == GROUPS - 1))
                return last

            pe.wait_ge(low_ready, lows(KT - 1))
            for g in range(GROUPS - 1):
                grouped(g)
            pe.wait_ge(params_loaded, PARAMS)
            for g in range(GROUPS - 2):
                layer1(g)
            grouped(GROUPS - 1)
            layer1(GROUPS - 2)
            layer1(GROUPS - 1).then_inc(l1_done, 1)
            pe.wait_ge(l1_relu, 1)
            nc.tensor.matmul(l2_ps[:, 0:QUARTER], w2_diag[:, :], l1_sb[:, :],
                             start=True, stop=True).then_inc(l2_done, 1)
            pe.wait_ge(l2_relu, 1)
            nc.tensor.matmul(l3_ps[0:QUARTERS, 0:QUARTER], w3_diag[:, :], l2_sb[:, :],
                             start=True, stop=True).then_inc(l3_done, 1)


def kernel(r_white_features, r_black_features, r_side_to_move, L0_rec_W_ft, L0_rec_W1, L0_rec_b1,
           L0_rec_W2, L0_rec_b2, L0_rec_W3, L0_rec_b3):
    import numpy as np
    import concourse.bacc as bacc
    from concourse.bass_utils import run_bass_kernel_spmd

    packed = np.concatenate([np.asarray(L0_rec_W_ft).T, np.asarray(r_white_features).T,
                             np.asarray(r_black_features).T], axis=1)
    laid = {
        "packed": packed,
        "side_to_move": np.asarray(r_side_to_move).reshape(QUARTERS, QUARTER),
        "w1t": np.asarray(L0_rec_W1).T,
        "b1": np.asarray(L0_rec_b1).reshape(L, 1),
        "w2t": np.asarray(L0_rec_W2).T,
        "b2": np.asarray(L0_rec_b2).reshape(L, 1),
        "w3t": np.asarray(L0_rec_W3).T,
        "b3": np.asarray(L0_rec_b3).reshape(1, 1),
    }
    nc = bacc.Bacc("TRN2", target_bir_lowering=False, num_devices=1)
    arrays, args = {}, []
    for name, a in laid.items():
        arrays[name] = np.ascontiguousarray(a)
        args.append(nc.dram_tensor(name, a.shape, mybir.dt.from_np(a.dtype), kind="ExternalInput").ap())
    out = nc.dram_tensor("out", (QUARTERS, QUARTER), mybir.dt.float32, kind="ExternalOutput").ap()
    feature_net_kernel(nc, *args, out)
    r = run_bass_kernel_spmd(nc, [arrays], core_ids=[0])
    return r.results[0]["out"].reshape(BATCH, 1)
```

```python
import concourse.bass as bass
from concourse import mybir
from contextlib import ExitStack

P = 128
BATCH = 512
IN = 5120
H = 256
L = 32
SIDES = 2
KT = IN // P
HB = H // P
ROW = H + SIDES * BATCH
RING = 8
TURNS = KT // RING
GROUPED = 4
QUARTERS = P // L
QUARTER = BATCH // QUARTERS
GROUPS = SIDES * HB
WAKE = 7

W_COLS = slice(0, H)
WHITE = slice(H, H + BATCH)
BLACK = slice(H + BATCH, ROW)
FINE = 4
PIECES = [[W_COLS, slice(H, H + BATCH // 2), slice(H + BATCH // 2, H + BATCH), BLACK]] \
    + [[W_COLS, WHITE, BLACK]] * (FINE - 1) + [[slice(0, ROW)]] * (RING - FINE)
EXTRA = sum(len(p) for p in PIECES) - RING


def split_through(t):
    if isinstance(t, int) and t < RING:
        return sum(len(p) for p in PIECES[:t + 1])
    return t + 1 + EXTRA


def feature_net_kernel(
    nc: bass.Bass,
    packed: bass.AP,
    side_to_move: bass.AP,
    w1t: bass.AP,
    b1: bass.AP,
    w2t: bass.AP,
    b2: bass.AP,
    w3t: bass.AP,
    b3: bass.AP,
    out: bass.AP,
):
    f32 = mybir.dt.float32
    f32r = mybir.dt.float32r
    bf16 = mybir.dt.bfloat16
    ALU = mybir.AluOpType
    ACT = mybir.ActivationFunctionType
    assert KT % RING == 0 and GROUPED <= RING and TURNS >= 3

    packed_v = packed.rearrange("(p t) n -> p t n", t=KT)

    ctx = ExitStack()
    with ctx:
        def sb(name, shape, dt=f32):
            return ctx.enter_context(nc.sbuf_tensor(name, shape, dt))

        def bank(name):
            return ctx.enter_context(nc.psum_tensor(name, [P, BATCH], f32))

        def sem(name):
            return ctx.enter_context(nc.semaphore(name))

        raw = sb("raw", [P, RING, ROW])
        high = sb("high", [P, RING, ROW], f32r)
        low = sb("low", [P, RING, ROW], f32r)
        zeros = sb("zeros", [P, BATCH], bf16)
        clipped = sb("clipped", [P, GROUPS, BATCH])
        w1_sb = sb("w1_sb", [P, GROUPS, L])
        w2_diag = sb("w2_diag", [P, P])
        w3_diag = sb("w3_diag", [P, QUARTERS])
        b1_col = sb("b1_col", [P, 1])
        b2_row = sb("b2_row", [1, QUARTERS, L])
        b3_row = sb("b3_row", [1, QUARTERS, 1])
        ones_row = sb("ones_row", [1, QUARTER])
        stm_sb = sb("stm_sb", [QUARTERS, QUARTER])
        l1_sb = sb("l1_sb", [P, QUARTER])
        l2_sb = sb("l2_sb", [P, QUARTER])
        out_sb = sb("out_sb", [QUARTERS, QUARTER])

        acc = [bank(f"acc{g}") for g in range(GROUPS)]
        l1_ps = bank("l1_ps")
        l2_ps = bank("l2_ps")
        l3_ps = bank("l3_ps")

        piece_loaded = [[sem(f"piece_loaded{t}_{i}") for i in range(len(PIECES[t]))] for t in range(FINE)]
        raw_loaded = [sem(f"raw_loaded{s}") for s in range(RING)]
        high_ready = sem("high_ready")
        low_ready = sem("low_ready")
        tile_used = sem("tile_used")
        consts_set = sem("consts_set")
        params_loaded = sem("params_loaded")
        zeros_ready = sem("zeros_ready")
        group_done = sem("group_done")
        clip_done = sem("clip_done")
        l1_done = sem("l1_done")
        l1_relu = sem("l1_relu")
        l2_done = sem("l2_done")
        l2_relu = sem("l2_relu")
        l3_done = sem("l3_done")
        row_done = sem("row_done")
        out_stored = sem("out_stored")
        block = ctx.enter_context(nc.Block())

        def loaded_before(s):
            return 0 if s < FINE else 16

        def quarter(q):
            return slice(q * QUARTER, (q + 1) * QUARTER)

        def parts(q):
            return slice(q * L, (q + 1) * L)

        @block.sync
        def _(sync):
            for s in range(RING):
                for i, cols in enumerate(PIECES[s]):
                    arrival = piece_loaded[s][i] if s < FINE else raw_loaded[s]
                    sync.dma_start(raw[:, s, cols], packed_v[:, s, cols]).then_inc(arrival, 16)
            with sync.Fori(1, TURNS) as turn:
                for s in range(RING):
                    sync.wait_ge(low_ready, split_through((turn - 1) * RING + s))
                    sync.dma_start(raw[:, s, :],
                                   packed_v[:, bass.ds(turn * RING + s, 1), :].rearrange("p t n -> p (t n)")
                                   ).then_inc(raw_loaded[s], 16)
            sync.wait_ge(row_done, 1)
            sync.dma_start(out, out_sb[:, :]).then_inc(out_stored, 16)
            sync.wait_ge(out_stored, 16)

        param_loads = [(w1_sb[:, :, :], w1t.rearrange("(g p) j -> p g j", p=P)),
                       (stm_sb[:, :], side_to_move),
                       (b2_row[:, :, :], b2.to_broadcast([1, QUARTERS, L])),
                       (b3_row[:, :, :], b3.to_broadcast([1, QUARTERS, 1]))]
        for q in range(QUARTERS):
            param_loads += [(w2_diag[parts(q), parts(q)], w2t), (w3_diag[parts(q), q:q + 1], w3t),
                            (b1_col[parts(q), :], b1)]
        PARAMS = 16 * len(param_loads)

        @block.gpsimd
        def _(gpsimd):
            nc.gpsimd.memset(w2_diag[:, :], 0.0).then_inc(consts_set, 1)
            nc.gpsimd.memset(w3_diag[:, :], 0.0).then_inc(consts_set, 1)
            nc.gpsimd.memset(ones_row[:, :], 1.0).then_inc(consts_set, 1)
            gpsimd.wait_ge(consts_set, 3)
            for dst, src in param_loads:
                gpsimd.dma_start(dst, src).then_inc(params_loaded, 16)

        @block.scalar
        def _(act):
            def split_high(s, cols=slice(0, ROW)):
                nc.scalar.activation(high[:, s, cols], raw[:, s, cols], ACT.Copy).then_inc(high_ready, 1)

            for s in range(RING):
                for i, cols in enumerate(PIECES[s]):
                    act.wait_ge(piece_loaded[s][i] if s < FINE else raw_loaded[s], 16)
                    split_high(s, cols)
            with act.Fori(1, TURNS) as turn:
                for s in range(RING):
                    act.wait_ge(raw_loaded[s], turn * 16 + loaded_before(s))
                    act.wait_ge(tile_used, (turn - 1) * RING + s + 1)
                    split_high(s)

        @block.vector
        def _(dve):
            def split_low(s, cols=slice(0, ROW)):
                nc.vector.tensor_tensor(low[:, s, cols], raw[:, s, cols], high[:, s, cols].bitcast(f32),
                                        ALU.subtract).then_inc(low_ready, 1)

            nc.vector.memset(zeros[:, :], 0.0).then_inc(zeros_ready, 1)
            pieces_done = 0
            for s in range(RING):
                for cols in PIECES[s]:
                    pieces_done += 1
                    dve.wait_ge(high_ready, pieces_done)
                    split_low(s, cols)
            with dve.Fori(1, TURNS) as turn:
                for s in range(RING):
                    dve.wait_ge(high_ready, split_through(turn * RING + s))
                    split_low(s)

            for g in range(GROUPS):
                dve.wait_ge(group_done, g + 1)
                for q in range(QUARTERS):
                    nc.vector.tensor_scalar(clipped[:, g, quarter(q)], acc[g][:, quarter(q)], 0.0, 1.0,
                                            ALU.max, ALU.min).then_inc(clip_done, 1)
            dve.wait_ge(l1_done, 1)
            nc.vector.tensor_scalar(l1_sb[:, :], l1_ps[:, 0:QUARTER], b1_col[:, :], 0.0,
                                    ALU.add, ALU.max).then_inc(l1_relu, 1)
            dve.wait_ge(l2_done, 1)
            nc.vector.tensor_scalar_max(l2_sb[:, :], l2_ps[:, 0:QUARTER], 0.0).then_inc(l2_relu, 1)
            dve.wait_ge(l3_done, 1)
            nc.vector.tensor_tensor(out_sb[:, :], l3_ps[0:QUARTERS, 0:QUARTER], stm_sb[:, :],
                                    ALU.mult).then_inc(row_done, 1)

        @block.tensor
        def _(pe):
            pe.wait_ge(zeros_ready, 1)
            for _ in range(WAKE - GROUPS):
                nc.tensor.matmul(l3_ps[:, :], zeros[:, 0:P], zeros[:, :], start=True, stop=True)
            for g in range(GROUPS):
                nc.tensor.matmul(acc[g][:, :], zeros[:, 0:P], zeros[:, :], start=True, stop=False)

            def product(s, side, hb, w, x, cols=slice(0, BATCH), stop=False):
                start = H + side * BATCH
                return nc.tensor.matmul(acc[side * HB + hb][:, cols], w[:, s, hb * P:(hb + 1) * P],
                                        x[:, s, start + cols.start:start + cols.stop],
                                        start=False, stop=stop)

            def tile(s):
                for hb in range(HB):
                    for x in (high, low):
                        for side in range(SIDES):
                            product(s, side, hb, high, x)
                    for side in range(SIDES):
                        last = product(s, side, hb, low, high)
                last.then_inc(tile_used, 1)

            def tile_in_pieces(s):
                before = split_through(s) - len(PIECES[s])
                features = PIECES[s][1:]
                for i, at in enumerate(features):
                    side, c = divmod(at.start - H, BATCH)
                    cols = slice(c, c + at.stop - at.start)
                    pe.wait_ge(high_ready, before + i + 2)
                    for hb in range(HB):
                        product(s, side, hb, high, high, cols)
                    if i == 0:
                        pe.wait_ge(low_ready, before + 1)
                    for hb in range(HB):
                        product(s, side, hb, low, high, cols)
                for i, at in enumerate(features):
                    side, c = divmod(at.start - H, BATCH)
                    cols = slice(c, c + at.stop - at.start)
                    pe.wait_ge(low_ready, before + i + 2)
                    for hb in range(HB):
                        last = product(s, side, hb, high, low, cols)
                last.then_inc(tile_used, 1)

            for s in range(FINE):
                tile_in_pieces(s)
            for s in range(FINE, RING):
                pe.wait_ge(low_ready, split_through(s))
                tile(s)
            with pe.Fori(1, TURNS - 1) as turn:
                for s in range(RING):
                    pe.wait_ge(low_ready, split_through(turn * RING + s))
                    tile(s)
            for s in range(RING - GROUPED):
                pe.wait_ge(low_ready, split_through(KT - RING + s))
                tile(s)

            def grouped(g):
                for s in range(RING - GROUPED, RING):
                    for w, x in ((high, high), (high, low), (low, high)):
                        last = product(s, g // HB, g % HB, w, x, stop=(w is low and s == RING - 1))
                last.then_inc(group_done, 1)

            def layer1(g):
                for q in range(QUARTERS):
                    pe.wait_ge(clip_done, g * QUARTERS + q + 1)
                    last = nc.tensor.matmul(l1_ps[parts(q), 0:QUARTER], w1_sb[:, g, :],
                                            clipped[:, g, quarter(q)],
                                            start=(g == 0), stop=(g == GROUPS - 1))
                return last

            def bias(ps, row, rows, stop=False):
                nc.tensor.matmul(ps[0:rows, 0:QUARTER], row[:, :, :].rearrange("o q l -> o (q l)"),
                                 ones_row[:, :], start=True, stop=stop)

            pe.wait_ge(low_ready, split_through(KT - 1))
            pe.wait_ge(params_loaded, PARAMS)
            for g in range(GROUPS):
                grouped(g)
            for g in range(GROUPS - 1):
                layer1(g)
            layer1(GROUPS - 1).then_inc(l1_done, 1)
            bias(l2_ps, b2_row, P)
            pe.wait_ge(l1_relu, 1)
            nc.tensor.matmul(l2_ps[:, 0:QUARTER], w2_diag[:, :], l1_sb[:, :],
                             start=False, stop=True).then_inc(l2_done, 1)
            bias(l3_ps, b3_row, QUARTERS)
            pe.wait_ge(l2_relu, 1)
            nc.tensor.matmul(l3_ps[0:QUARTERS, 0:QUARTER], w3_diag[:, :], l2_sb[:, :],
                             start=False, stop=True).then_inc(l3_done, 1)


def kernel(r_white_features, r_black_features, r_side_to_move, L0_rec_W_ft, L0_rec_W1, L0_rec_b1,
           L0_rec_W2, L0_rec_b2, L0_rec_W3, L0_rec_b3):
    import numpy as np
    import concourse.bacc as bacc
    from concourse.bass_utils import run_bass_kernel_spmd

    packed = np.concatenate([np.asarray(L0_rec_W_ft).T, np.asarray(r_white_features).T,
                             np.asarray(r_black_features).T], axis=1)
    laid = {
        "packed": packed,
        "side_to_move": np.asarray(r_side_to_move).reshape(QUARTERS, QUARTER),
        "w1t": np.asarray(L0_rec_W1).T,
        "b1": np.asarray(L0_rec_b1).reshape(L, 1),
        "w2t": np.asarray(L0_rec_W2).T,
        "b2": np.asarray(L0_rec_b2).reshape(1, 1, L),
        "w3t": np.asarray(L0_rec_W3).T,
        "b3": np.asarray(L0_rec_b3).reshape(1, 1, 1),
    }
    nc = bacc.Bacc("TRN2", target_bir_lowering=False, num_devices=1)
    arrays, args = {}, []
    for name, a in laid.items():
        arrays[name] = np.ascontiguousarray(a)
        args.append(nc.dram_tensor(name, a.shape, mybir.dt.from_np(a.dtype), kind="ExternalInput").ap())
    out = nc.dram_tensor("out", (QUARTERS, QUARTER), mybir.dt.float32, kind="ExternalOutput").ap()
    feature_net_kernel(nc, *args, out)
    r = run_bass_kernel_spmd(nc, [arrays], core_ids=[0])
    return r.results[0]["out"].reshape(BATCH, 1)
```
